# Optimizing a Trainium2 kernel written in Bass

```python
import numpy as np
import jax
import jax.numpy as jnp

def _softmax(x, axis=-1):
    return jax.nn.softmax(x, axis=axis)

def _gelu(x):
    return jax.nn.gelu(x, approximate=True)

def _silu(x):
    return jax.nn.silu(x)

def _sigmoid(x):
    return jax.nn.sigmoid(x)

def _layernorm(x, axis=-1, eps=1e-05):
    m = jnp.mean(x, axis=axis, keepdims=True)
    v = jnp.var(x, axis=axis, keepdims=True)
    return (x - m) / jnp.sqrt(v + eps)

def _scatter_add(tgt, idx, src, axis=0):
    return tgt.at[idx].add(src)

def _segment_sum(src, seg, n):
    return jax.ops.segment_sum(src, seg, n)
kernel_name = 'mk_dlrm_tower_d1_rec_r8_050d6a'

def setup_inputs(seed: int=0):
    np.random.seed(seed)
    _w = jnp.asarray

    def _rec_inputs():
        import jax
        import jax.numpy as jnp
        _tk = jax.random.key(seed)
        dense_ctx = jax.random.normal(jax.random.fold_in(_tk, 190), (512, 16), jnp.float32)
        ids = jnp.stack([jax.random.randint(jax.random.fold_in(_tk, 200 + f), (512,), 0, v, jnp.int32) for f, v in enumerate([1000, 125000, 1250, 12500, 12500, 1250, 125000, 1250, 1000, 1000, 1000, 125000, 12500, 1250, 1250, 1000, 1000, 1250, 1000, 12500, 1250, 1250, 12500, 1000, 12500, 1250, 1250, 12500, 1250, 1250, 1000, 1000])], axis=1)
        tbl_0 = 0.05 * jax.random.normal(jax.random.fold_in(_tk, 500 + 0), (1000, 64), jnp.float32)
        tbl_1 = 0.05 * jax.random.normal(jax.random.fold_in(_tk, 500 + 1), (125000, 64), jnp.float32)
        tbl_2 = 0.05 * jax.random.normal(jax.random.fold_in(_tk, 500 + 2), (1250, 64), jnp.float32)
        tbl_3 = 0.05 * jax.random.normal(jax.random.fold_in(_tk, 500 + 3), (12500, 64), jnp.float32)
        tbl_4 = 0.05 * jax.random.normal(jax.random.fold_in(_tk, 500 + 4), (12500, 64), jnp.float32)
        tbl_5 = 0.05 * jax.random.normal(jax.random.fold_in(_tk, 500 + 5), (1250, 64), jnp.float32)
        tbl_6 = 0.05 * jax.random.normal(jax.random.fold_in(_tk, 500 + 6), (125000, 64), jnp.float32)
        tbl_7 = 0.05 * jax.random.normal(jax.random.fold_in(_tk, 500 + 7), (1250, 64), jnp.float32)
        tbl_8 = 0.05 * jax.random.normal(jax.random.fold_in(_tk, 500 + 8), (1000, 64), jnp.float32)
        tbl_9 = 0.05 * jax.random.normal(jax.random.fold_in(_tk, 500 + 9), (1000, 64), jnp.float32)
        tbl_10 = 0.05 * jax.random.normal(jax.random.fold_in(_tk, 500 + 10), (1000, 64), jnp.float32)
        tbl_11 = 0.05 * jax.random.normal(jax.random.fold_in(_tk, 500 + 11), (125000, 64), jnp.float32)
        tbl_12 = 0.05 * jax.random.normal(jax.random.fold_in(_tk, 500 + 12), (12500, 64), jnp.float32)
        tbl_13 = 0.05 * jax.random.normal(jax.random.fold_in(_tk, 500 + 13), (1250, 64), jnp.float32)
        tbl_14 = 0.05 * jax.random.normal(jax.random.fold_in(_tk, 500 + 14), (1250, 64), jnp.float32)
        tbl_15 = 0.05 * jax.random.normal(jax.random.fold_in(_tk, 500 + 15), (1000, 64), jnp.float32)
        tbl_16 = 0.05 * jax.random.normal(jax.random.fold_in(_tk, 500 + 16), (1000, 64), jnp.float32)
        tbl_17 = 0.05 * jax.random.normal(jax.random.fold_in(_tk, 500 + 17), (1250, 64), jnp.float32)
        tbl_18 = 0.05 * jax.random.normal(jax.random.fold_in(_tk, 500 + 18), (1000, 64), jnp.float32)
        tbl_19 = 0.05 * jax.random.normal(jax.random.fold_in(_tk, 500 + 19), (12500, 64), jnp.float32)
        tbl_20 = 0.05 * jax.random.normal(jax.random.fold_in(_tk, 500 + 20), (1250, 64), jnp.float32)
        tbl_21 = 0.05 * jax.random.normal(jax.random.fold_in(_tk, 500 + 21), (1250, 64), jnp.float32)
        tbl_22 = 0.05 * jax.random.normal(jax.random.fold_in(_tk, 500 + 22), (12500, 64), jnp.float32)
        tbl_23 = 0.05 * jax.random.normal(jax.random.fold_in(_tk, 500 + 23), (1000, 64), jnp.float32)
        tbl_24 = 0.05 * jax.random.normal(jax.random.fold_in(_tk, 500 + 24), (12500, 64), jnp.float32)
        tbl_25 = 0.05 * jax.random.normal(jax.random.fold_in(_tk, 500 + 25), (1250, 64), jnp.float32)
        tbl_26 = 0.05 * jax.random.normal(jax.random.fold_in(_tk, 500 + 26), (1250, 64), jnp.float32)
        tbl_27 = 0.05 * jax.random.normal(jax.random.fold_in(_tk, 500 + 27), (12500, 64), jnp.float32)
        tbl_28 = 0.05 * jax.random.normal(jax.random.fold_in(_tk, 500 + 28), (1250, 64), jnp.float32)
        tbl_29 = 0.05 * jax.random.normal(jax.random.fold_in(_tk, 500 + 29), (1250, 64), jnp.float32)
        tbl_30 = 0.05 * jax.random.normal(jax.random.fold_in(_tk, 500 + 30), (1000, 64), jnp.float32)
        tbl_31 = 0.05 * jax.random.normal(jax.random.fold_in(_tk, 500 + 31), (1000, 64), jnp.float32)
        _rk = jax.random.fold_in(_tk, 7)
        W_top1 = 0.0441942 * jax.random.normal(jax.random.fold_in(_tk, 801), (512, 512), jnp.float32)
        W_top2 = 0.0441942 * jax.random.normal(jax.random.fold_in(_tk, 802), (512, 256), jnp.float32)
        W_top3 = 0.0625 * jax.random.normal(jax.random.fold_in(_tk, 803), (256, 1), jnp.float32)
        b_top1 = jnp.zeros((512,), jnp.float32)
        b_top2 = jnp.zeros((256,), jnp.float32)
        return (dense_ctx, ids, tbl_0, tbl_1, tbl_2, tbl_3, tbl_4, tbl_5, tbl_6, tbl_7, tbl_8, tbl_9, tbl_10, tbl_11, tbl_12, tbl_13, tbl_14, tbl_15, tbl_16, tbl_17, tbl_18, tbl_19, tbl_20, tbl_21, tbl_22, tbl_23, tbl_24, tbl_25, tbl_26, tbl_27, tbl_28, tbl_29, tbl_30, tbl_31, W_top1, b_top1, W_top2, b_top2, W_top3)
    dense_ctx, ids, tbl_0, tbl_1, tbl_2, tbl_3, tbl_4, tbl_5, tbl_6, tbl_7, tbl_8, tbl_9, tbl_10, tbl_11, tbl_12, tbl_13, tbl_14, tbl_15, tbl_16, tbl_17, tbl_18, tbl_19, tbl_20, tbl_21, tbl_22, tbl_23, tbl_24, tbl_25, tbl_26, tbl_27, tbl_28, tbl_29, tbl_30, tbl_31, W_top1, b_top1, W_top2, b_top2, W_top3 = _rec_inputs()

    def _L0_rec_setup():
        import jax, jax.numpy as jnp
        import numpy as np
        B, F, E = (512, 32, 64)
        P = F * (F - 1) // 2
        key = jax.random.key(seed)
        k1, k2 = jax.random.split(key)
        x = jax.random.normal(k1, (B, F, E), dtype=jnp.float32)
        kernel = jax.random.normal(k2, (E, P, E), dtype=jnp.float32) * 0.05
        return {'x': x, 'kernel': kernel}
    _L0_rec_all = _L0_rec_setup()
    _L0_rec_in = {k: v for k, v in _L0_rec_all.items() if k in ('kernel',)}
    del _L0_rec_all
    return {'dense_ctx': dense_ctx, 'ids': ids, 'tbl_0': tbl_0, 'tbl_1': tbl_1, 'tbl_2': tbl_2, 'tbl_3': tbl_3, 'tbl_4': tbl_4, 'tbl_5': tbl_5, 'tbl_6': tbl_6, 'tbl_7': tbl_7, 'tbl_8': tbl_8, 'tbl_9': tbl_9, 'tbl_10': tbl_10, 'tbl_11': tbl_11, 'tbl_12': tbl_12, 'tbl_13': tbl_13, 'tbl_14': tbl_14, 'tbl_15': tbl_15, 'tbl_16': tbl_16, 'tbl_17': tbl_17, 'tbl_18': tbl_18, 'tbl_19': tbl_19, 'tbl_20': tbl_20, 'tbl_21': tbl_21, 'tbl_22': tbl_22, 'tbl_23': tbl_23, 'tbl_24': tbl_24, 'tbl_25': tbl_25, 'tbl_26': tbl_26, 'tbl_27': tbl_27, 'tbl_28': tbl_28, 'tbl_29': tbl_29, 'tbl_30': tbl_30, 'tbl_31': tbl_31, 'W_top1': W_top1, 'b_top1': b_top1, 'W_top2': W_top2, 'b_top2': b_top2, 'W_top3': W_top3, 'L0_rec_kernel': _L0_rec_in['kernel']}

def reference(dense_ctx, ids, tbl_0, tbl_1, tbl_2, tbl_3, tbl_4, tbl_5, tbl_6, tbl_7, tbl_8, tbl_9, tbl_10, tbl_11, tbl_12, tbl_13, tbl_14, tbl_15, tbl_16, tbl_17, tbl_18, tbl_19, tbl_20, tbl_21, tbl_22, tbl_23, tbl_24, tbl_25, tbl_26, tbl_27, tbl_28, tbl_29, tbl_30, tbl_31, W_top1, b_top1, W_top2, b_top2, W_top3, L0_rec_kernel):
    import jax
    import jax.numpy as jnp

    def _L0_rec_ref(x, kernel):
        import jax, jax.numpy as jnp
        import numpy as np
        B, F, E = (512, 32, 64)
        P = F * (F - 1) // 2
        nf = x.shape[1]
        row_idx, col_idx = np.triu_indices(nf, k=1)
        p = x[:, row_idx, :]
        q = x[:, col_idx, :]
        kp = jnp.einsum('bpe,fpe,bpf->bp', p, kernel, q)
        return kp
    e = jnp.stack([tbl_0[ids[:, 0]], tbl_1[ids[:, 1]], tbl_2[ids[:, 2]], tbl_3[ids[:, 3]], tbl_4[ids[:, 4]], tbl_5[ids[:, 5]], tbl_6[ids[:, 6]], tbl_7[ids[:, 7]], tbl_8[ids[:, 8]], tbl_9[ids[:, 9]], tbl_10[ids[:, 10]], tbl_11[ids[:, 11]], tbl_12[ids[:, 12]], tbl_13[ids[:, 13]], tbl_14[ids[:, 14]], tbl_15[ids[:, 15]], tbl_16[ids[:, 16]], tbl_17[ids[:, 17]], tbl_18[ids[:, 18]], tbl_19[ids[:, 19]], tbl_20[ids[:, 20]], tbl_21[ids[:, 21]], tbl_22[ids[:, 22]], tbl_23[ids[:, 23]], tbl_24[ids[:, 24]], tbl_25[ids[:, 25]], tbl_26[ids[:, 26]], tbl_27[ids[:, 27]], tbl_28[ids[:, 28]], tbl_29[ids[:, 29]], tbl_30[ids[:, 30]], tbl_31[ids[:, 31]]], axis=1)
    z = _L0_rec_ref(e, L0_rec_kernel)
    z = z.reshape(z.shape[0], -1)
    h = jnp.concatenate([z, dense_ctx], axis=1)
    h = jnp.maximum(h @ W_top1 + b_top1, 0.0)
    h = jnp.maximum(h @ W_top2 + b_top2, 0.0)
    y = h @ W_top3
    return y

_drawn_inputs = setup_inputs


def setup_inputs(seed=0):
    import zlib

    import numpy as np

    out = dict(_drawn_inputs(seed))
    spreads = {'b_top1': (0.0, 0.1), 'b_top2': (0.0, 0.1)}
    factors = {'tbl_0': 6.68,
     'tbl_1': 5.978,
     'tbl_2': 5.635,
     'tbl_3': 6.164,
     'tbl_4': 5.24,
     'tbl_5': 6.349,
     'tbl_6': 5.842,
     'tbl_7': 4.76,
     'tbl_8': 5.437,
     'tbl_9': 5.521,
     'tbl_10': 5.724,
     'tbl_11': 5.631,
     'tbl_12': 5.28,
     'tbl_13': 5.553,
     'tbl_14': 6.054,
     'tbl_15': 5.607,
     'tbl_16': 5.095,
     'tbl_17': 6.32,
     'tbl_18': 5.005,
     'tbl_19': 5.764,
     'tbl_20': 5.31,
     'tbl_21': 5.866,
     'tbl_22': 5.913,
     'tbl_23': 6.069,
     'tbl_24': 6.129,
     'tbl_25': 5.654,
     'tbl_26': 5.713,
     'tbl_27': 5.802,
     'tbl_28': 6.291,
     'tbl_29': 5.777,
     'tbl_30': 5.771,
     'tbl_31': 6.511}
    for name, (base, spread) in spreads.items():
        noise = np.random.default_rng([zlib.crc32(name.encode()), seed]).standard_normal(out[name].shape)
        drawn = base * np.exp(spread * noise) if base else spread * noise
        out[name] = jnp.asarray(drawn.astype(out[name].dtype))
    for name, factor in factors.items():
        out[name] = (out[name] * factor).astype(out[name].dtype)
    return out
```

```python
from contextlib import ExitStack

import numpy as np

import concourse.bass as bass
from concourse import mybir

B, F, E = 512, 32, 64
NDENSE = 16
H1, H2 = 512, 256
P = 128
TB = B // P
NJ = F // 2
NBANK = 4
STRIPS = 4
COUPLE_GROUPS = 15
GROUPS = COUPLE_GROUPS + 1
CHUNK_GROUPS = 2
CHUNKS = GROUPS // CHUNK_GROUPS
GW = 4 * P
SW = 4 * E
BANK_W = COUPLE_GROUPS * GW + SW


def pair_index(i, j):
    return i * (2 * F - i - 1) // 2 + j - i - 1


def blocks():
    return [(m, J) for J in range(1, NJ) for m in range(J)]


def single_m(bank, strip):
    return STRIPS * bank + strip


def bank_pairs(bank):
    out = []
    for m, J in blocks()[2 * COUPLE_GROUPS * bank:2 * COUPLE_GROUPS * (bank + 1)]:
        for j in (2 * J, 2 * J + 1):
            out += [pair_index(2 * m, j), pair_index(2 * m + 1, j)]
    return out + [pair_index(2 * m, 2 * m + 1) for m in (single_m(bank, s) for s in range(STRIPS))]


def z_rows(bank):
    pairs = bank_pairs(bank)
    row = np.zeros(P, np.int64)
    for c in range(STRIPS):
        for r in range(COUPLE_GROUPS):
            for h in range(2):
                row[32 * c + 2 * r + h] = pairs[8 * r + 2 * c + h]
        row[32 * c + 30] = pairs[8 * COUPLE_GROUPS + c]
        row[32 * c + 31] = F * (F - 1) // 2 + STRIPS * bank + c
    return row


def build(nc, ids, tables, kern, dense, w1, b1, w2, b2, w3, sel, place, ident_d, out):
    F32, F32R, I32 = mybir.dt.float32, mybir.dt.float32r, mybir.dt.int32
    ALU, ACT = mybir.AluOpType, mybir.ActivationFunctionType
    XG, XS, KR, KS, TS = 4, 2, 3, 3, 2
    BLOCKS = blocks()

    ctx = ExitStack()
    with ctx:
        def sb(name, shape, dt=F32):
            return ctx.enter_context(nc.sbuf_tensor(name, shape, dt))

        def sem(name):
            return ctx.enter_context(nc.semaphore(name))

        ids_sb = sb("ids_sb", [P, TB, F], I32)
        gathered = sb("gathered", [P, XG, TB, 2 * E])
        split = sb("split", [P, XS, TB, 2, 2 * E], F32R)
        moving = sb("moving", [P, F, B], F32R)
        factor = sb("factor", [P, NJ, B])
        k_raw = sb("k_raw", [P, KR, CHUNK_GROUPS * GW])
        h1_sb = k_raw[:, 0:2, :].rearrange("p s (m b) -> p (s m) b", b=B)
        h2_sb = k_raw[:, 2, :].rearrange("p (m b) -> p m b", b=B)
        k_hi = sb("k_hi", [P, KS, CHUNK_GROUPS * GW], F32R)
        k_lo = sb("k_lo", [P, KS, CHUNK_GROUPS * GW], F32R)
        prod = sb("prod", [P, TS, 4, B])
        z_sb = sb("z_sb", [P, NBANK, B])
        y_sb = sb("y_sb", [1, B])
        w1_sb = sb("w1_sb", [P, NBANK, H1])
        w2_sb = sb("w2_sb", [P, H1 // P, H2])
        w3_sb = sb("w3_sb", [P, H2 // P])
        b1_sb = sb("b1_sb", [P, H1 // P])
        b2_sb = sb("b2_sb", [P, H2 // P])
        dense_sb = sb("dense_sb", [STRIPS, NBANK, B])
        place_sb = sb("place_sb", [STRIPS, P])
        sel_sb = sb("sel_sb", [P, 2, 62])
        ident = sb("ident", [P, P])
        ident_r = sb("ident_r", [P, P], F32R)

        u_ps = [ctx.enter_context(nc.psum_tensor(f"u_ps{i}", [P, 2, B], F32)) for i in range(2)]
        z_ps = [ctx.enter_context(nc.psum_tensor(f"z_ps{i}", [P, B], F32)) for i in range(2)]
        t_ps = [ctx.enter_context(nc.psum_tensor(f"t_ps{i}", [P, B], F32)) for i in range(2)]

        ids_in = sem("ids_in")
        const_in = sem("const_in")
        weights_in = sem("weights_in")
        field_in = [sem(f"field_in{J}") for J in range(NJ)]
        k_in = [sem(f"k_in{i}") for i in range(KR)]
        ident_ready = sem("ident_ready")
        k_hi_ready = sem("k_hi_ready")
        k_lo_ready = sem("k_lo_ready")
        x_hi_ready = sem("x_hi_ready")
        x_lo_ready = sem("x_lo_ready")
        turned = sem("turned")
        x_ready = sem("x_ready")
        u_ready = sem("u_ready")
        prod_ready = sem("prod_ready")
        summed = sem("summed")
        z_ready = sem("z_ready")
        h1_done = sem("h1_done")
        h1_ready = sem("h1_ready")
        h2_done = sem("h2_done")
        h2_ready = sem("h2_ready")
        y_done = sem("y_done")
        y_ready = sem("y_ready")
        y_out = sem("y_out")

        NG = NBANK * GROUPS

        def group_blocks(g):
            k, r = divmod(g, GROUPS)
            if r < COUPLE_GROUPS:
                two = BLOCKS[2 * (COUPLE_GROUPS * k + r):][:2]
                return [(m, (2 * J, 2 * J + 1)) for m, J in two]
            return [(single_m(k, s), (2 * single_m(k, s) + 1, 2 * single_m(k, s) + 3)) for s in (0, 2)]

        def last_stage(g):
            return max(j // 2 for _, js in group_blocks(g) for j in js)

        steps, staged = [("chunk", 0), ("stage", 0)], 0
        for g in range(NG):
            need = last_stage(g)
            ahead = max([need] + [last_stage(q) for q in range(g, min(g + 2, NG))])
            while staged < ahead:
                staged += 1
                steps.append(("stage", staged))
            if g % CHUNK_GROUPS == 0 and g // CHUNK_GROUPS + 1 < NG // CHUNK_GROUPS:
                steps.append(("chunk", g // CHUNK_GROUPS + 1))
            steps.append(("group", g))
            if g:
                steps.append(("sum", g - 1))
                if g % GROUPS == 0:
                    steps.append(("bank", g // GROUPS - 1))
        steps += [("sum", NG - 1), ("bank", NBANK - 1)]

        def chunk_width(n):
            return CHUNK_GROUPS * GW if (n + 1) % CHUNKS else (CHUNK_GROUPS - 1) * GW + SW

        def columns(g):
            return (g % CHUNK_GROUPS) * GW, (P if g % GROUPS < COUPLE_GROUPS else E)

        def h1_ps(m):
            return (t_ps[0][:, :], t_ps[1][:, :], z_ps[0][:, :], u_ps[0][:, 0, :])[m]

        block = ctx.enter_context(nc.Block())

        @block.sync
        def _(sp):
            sp.dma_start(ident[:, :], ident_d).then_inc(const_in, 16)
            sp.dma_start(sel_sb[:, :, :], sel).then_inc(const_in, 16)
            sp.dma_start(place_sb[:, :], place).then_inc(const_in, 16)
            sp.dma_start(dense_sb[:, :, :], dense).then_inc(const_in, 16)
            for n in range(NBANK * CHUNKS):
                at = (n // CHUNKS) * BANK_W + (n % CHUNKS) * CHUNK_GROUPS * GW
                if n >= KR:
                    sp.wait_ge(k_lo_ready, n - KR + 1)
                for half in range(2):
                    sp.dma_start(k_raw[half * E:(half + 1) * E, n % KR, 0:chunk_width(n)],
                                 kern[:, at:at + chunk_width(n)]).then_inc(k_in[n % KR], 16)
                if n == 4:
                    sp.dma_start(w1_sb[:, :, :], w1).then_inc(weights_in, 16)
                    sp.dma_start(w2_sb[:, :, :], w2).then_inc(weights_in, 16)
                    sp.dma_start(w3_sb[:, :], w3).then_inc(weights_in, 16)
                    sp.dma_start(b1_sb[:, :], b1).then_inc(weights_in, 16)
                    sp.dma_start(b2_sb[:, :], b2).then_inc(weights_in, 16)
            sp.wait_ge(y_ready, 1)
            sp.dma_start(out, y_sb[:, :]).then_inc(y_out, 16)
            sp.wait_ge(y_out, 16)

        @block.gpsimd
        def _(pool):
            pool.dma_start(ids_sb[:, :, :], ids).then_inc(ids_in, 16)
            pool.wait_ge(ids_in, 16)
            for J in range(NJ):
                if J >= XG:
                    pool.wait_ge(x_lo_ready, J - XG + 1)
                    pool.wait_ge(turned, 3 * (J - XG + 1))
                for t in range(TB):
                    for h in range(2):
                        f = 2 * J + h
                        pool.indirect_dma_start(
                            gathered[:, J % XG, t, h * E:(h + 1) * E], None, tables[f],
                            bass.IndirectOffsetOnAxis(ap=ids_sb[:, t, f:f + 1], axis=0),
                        ).then_inc(field_in[J], 16)

        @block.scalar
        def _(act):
            act.wait_ge(const_in, 4 * 16)
            act.copy(ident_r[:, :], ident[:, :]).then_inc(ident_ready, 1)
            for what, n in steps:
                if what == "chunk":
                    w = chunk_width(n)
                    act.wait_ge(k_in[n % KR], 32 * (n // KR + 1))
                    if n >= KS:
                        act.wait_ge(u_ready, 2 * CHUNK_GROUPS * (n - KS + 1))
                    act.copy(k_hi[:, n % KS, 0:w], k_raw[:, n % KR, 0:w]).then_inc(k_hi_ready, 1)
                elif what == "stage":
                    act.wait_ge(field_in[n], 2 * TB * 16)
                    if n >= XS:
                        act.wait_ge(turned, 3 * (n - XS + 1))
                    act.copy(split[:, n % XS, :, :, 0:E],
                             gathered[:, n % XG, :, :].rearrange("p t (h e) -> p t h e", h=2)).then_inc(x_hi_ready, 1)
                    for q in range(3):
                        act.wait_ge(turned, 3 * n + q + 1)
                        to = moving[:, 2 * n + q, :] if q < 2 else factor[:, n, :]
                        act.copy(to, t_ps[(3 * n + q) % 2][:, :]).then_inc(x_ready, 1)
                elif what == "bank":
                    act.wait_ge(summed, GROUPS * (n + 1))
                    act.copy(z_sb[:, n, :], z_ps[n % 2][:, :]).then_inc(z_ready, 1)
            act.wait_ge(weights_in, 5 * 16)
            for m in range(H1 // P):
                act.wait_ge(h1_done, m + 1)
                act.activation(h1_sb[:, m, :], h1_ps(m), ACT.Relu, bias=b1_sb[:, m:m + 1]).then_inc(h1_ready, 1)
            for m in range(H2 // P):
                act.wait_ge(h2_done, m + 1)
                act.activation(h2_sb[:, m, :], u_ps[1][:, m, :], ACT.Relu, bias=b2_sb[:, m:m + 1]).then_inc(h2_ready, 1)
            act.wait_ge(y_done, 1)
            act.copy(y_sb[:, :], t_ps[0][0:1, :]).then_inc(y_ready, 1)

        @block.vector
        def _(dve):
            for what, n in steps:
                if what == "chunk":
                    w = chunk_width(n)
                    dve.wait_ge(k_hi_ready, n + 1)
                    dve.tensor_tensor(k_lo[:, n % KS, 0:w], k_raw[:, n % KR, 0:w],
                                      k_hi[:, n % KS, 0:w].bitcast(F32), ALU.subtract).then_inc(k_lo_ready, 1)
                elif what == "stage":
                    dve.wait_ge(x_hi_ready, n + 1)
                    dve.tensor_tensor(split[:, n % XS, :, :, E:2 * E],
                                      gathered[:, n % XG, :, :].rearrange("p t (h e) -> p t h e", h=2),
                                      split[:, n % XS, :, :, 0:E].bitcast(F32), ALU.subtract).then_inc(x_lo_ready, 1)
                elif what == "group":
                    rows = P if n % GROUPS < COUPLE_GROUPS else E
                    for h, (m, js) in enumerate(group_blocks(n)):
                        bl = 2 * n + h
                        dve.wait_ge(u_ready, bl + 1)
                        dve.wait_ge(x_ready, 3 * (max(js) // 2 + 1))
                        if n >= TS:
                            dve.wait_ge(summed, n - TS + 1)
                        if rows == P:
                            by = factor[:, m:m + 1, :].to_broadcast([P, 2, B])
                        else:
                            by = factor[0:rows, m:m + 2, :]
                        dve.tensor_tensor(prod[0:rows, n % TS, 2 * h:2 * h + 2, :], u_ps[bl % 2][0:rows, :, :],
                                          by, ALU.mult).then_inc(prod_ready, 1)

        @block.tensor
        def _(pe):
            pe.wait_ge(ident_ready, 1)
            for what, n in steps:
                if what == "stage":
                    pe.wait_ge(x_lo_ready, n + 1)
                    for q in range(3):
                        if 3 * n + q >= 2:
                            pe.wait_ge(x_ready, 3 * n + q - 1)
                        to = t_ps[(3 * n + q) % 2]
                        for t in range(TB):
                            if q < 2:
                                last = pe.transpose(to[:, t * P:(t + 1) * P].bitcast(F32R), split[:, n % XS, t, q, :],
                                                    ident_r[:, :])
                            else:
                                last = pe.transpose(to[:, t * P:(t + 1) * P], gathered[:, n % XG, t, :], ident[:, :])
                        last.then_inc(turned, 1)
                elif what == "group":
                    k, r = divmod(n, GROUPS)
                    slot = n // CHUNK_GROUPS % KS
                    first, width = columns(n)
                    pe.wait_ge(k_lo_ready, n // CHUNK_GROUPS + 1)
                    pe.wait_ge(x_ready, 3 * (last_stage(n) + 1))
                    if r == 0:
                        if k >= 2:
                            pe.wait_ge(z_ready, k - 1)
                        pe.matmul(z_ps[k % 2][:, :], place_sb[:, :], dense_sb[:, k, :], start=True, stop=False)
                    for h, (m, js) in enumerate(group_blocks(n)):
                        bl = 2 * n + h
                        if bl >= 2:
                            pe.wait_ge(prod_ready, bl - 1)
                        for c, j in enumerate(js):
                            at = first + (2 * h + c) * width
                            pe.matmul(u_ps[bl % 2][0:width, c, :], k_hi[:, slot, at:at + width], moving[:, j, :],
                                      start=True, stop=False)
                            last = pe.matmul(u_ps[bl % 2][0:width, c, :], k_lo[:, slot, at:at + width], moving[:, j, :],
                                             start=False, stop=True)
                        last.then_inc(u_ready, 1)
                elif what == "sum":
                    k, r = divmod(n, GROUPS)
                    single = r == COUPLE_GROUPS
                    rows = E if single else P
                    pe.wait_ge(prod_ready, 2 * n + 2)
                    if n == NG - 1:
                        pe.wait_ge(weights_in, 5 * 16)
                        pe.wait_ge(z_ready, NBANK - 1)
                        for m in range(H1 // P):
                            for kk in range(NBANK - 1):
                                pe.matmul(h1_ps(m), w1_sb[:, kk, m * P:(m + 1) * P], z_sb[:, kk, :],
                                          start=kk == 0, stop=False)
                    for c in range(STRIPS):
                        s = sel_sb[0:rows, 1, 1:33] if single else sel_sb[0:rows, 0, 30 - 2 * r:62 - 2 * r]
                        last = pe.matmul(z_ps[k % 2][32 * c:32 * c + 32, :], s, prod[0:rows, n % TS, c, :],
                                         start=False, stop=single)
                    last.then_inc(summed, 1)
            pe.wait_ge(z_ready, NBANK)
            for m in range(H1 // P):
                pe.matmul(h1_ps(m), w1_sb[:, NBANK - 1, m * P:(m + 1) * P], z_sb[:, NBANK - 1, :],
                          start=False, stop=True).then_inc(h1_done, 1)
            for m in range(H2 // P):
                for kk in range(H1 // P):
                    pe.wait_ge(h1_ready, kk + 1)
                    last = pe.matmul(u_ps[1][:, m, :], w2_sb[:, kk, m * P:(m + 1) * P], h1_sb[:, kk, :],
                                     start=kk == 0, stop=kk == H1 // P - 1)
                last.then_inc(h2_done, 1)
            for kk in range(H2 // P):
                pe.wait_ge(h2_ready, kk + 1)
                last = pe.matmul(t_ps[0][0:1, :], w3_sb[:, kk:kk + 1], h2_sb[:, kk, :],
                                 start=kk == 0, stop=kk == H2 // P - 1)
            last.then_inc(y_done, 1)


def kernel(**inputs):
    import concourse.bacc as _bacc
    from concourse.bass_utils import run_bass_kernel_spmd as _run

    a = {k: np.asarray(v) for k, v in inputs.items()}
    order = np.concatenate([bank_pairs(k) for k in range(NBANK)])
    kt = a["L0_rec_kernel"][:, order, :].reshape(E, NBANK * BANK_W)
    rows = np.concatenate([z_rows(k) for k in range(NBANK)])

    sel = np.zeros((P, 2, 62), np.float32)
    sel[:E, 0, 30] = 1
    sel[E:, 0, 31] = 1
    sel[:E, 1, 31] = 1
    place = np.zeros((STRIPS, P), np.float32)
    for c in range(STRIPS):
        place[c, 32 * c + 31] = 1

    arrays = {
        "ids": a["ids"].reshape(TB, P, F).transpose(1, 0, 2),
        **{f"tbl_{f}": a[f"tbl_{f}"] for f in range(F)},
        "kern": kt,
        "dense": a["dense_ctx"].T.reshape(NBANK, STRIPS, B).transpose(1, 0, 2),
        "w1": a["W_top1"][rows].reshape(NBANK, P, H1).transpose(1, 0, 2),
        "b1": a["b_top1"].reshape(H1 // P, P).T,
        "w2": a["W_top2"].reshape(H1 // P, P, H2).transpose(1, 0, 2),
        "b2": a["b_top2"].reshape(H2 // P, P).T,
        "w3": a["W_top3"].reshape(H2 // P, P).T,
        "sel": sel, "place": place, "ident": np.eye(P, dtype=np.float32),
    }
    arrays = {f"in_{k}": np.ascontiguousarray(v) for k, v in arrays.items()}
    nc = _bacc.Bacc("TRN2", target_bir_lowering=False, num_devices=1)
    ap = {k: nc.dram_tensor(k, v.shape, mybir.dt.from_np(v.dtype), kind="ExternalInput").ap() for k, v in arrays.items()}
    out = nc.dram_tensor("out_y", (1, B), mybir.dt.float32, kind="ExternalOutput").ap()
    build(nc, ap["in_ids"], [ap[f"in_tbl_{f}"] for f in range(F)], ap["in_kern"], ap["in_dense"], ap["in_w1"],
          ap["in_b1"], ap["in_w2"], ap["in_b2"], ap["in_w3"], ap["in_sel"], ap["in_place"], ap["in_ident"], out)
    r = _run(nc, [arrays], core_ids=[0])
    return r.results[0]["out_y"].reshape(B, 1)
```

```python
from contextlib import ExitStack

import numpy as np

import concourse.bass as bass
from concourse import mybir

B, F, E = 512, 32, 64
ROWS = [1000, 125000, 1250, 12500, 12500, 1250, 125000, 1250, 1000, 1000, 1000, 125000, 12500, 1250, 1250, 1000,
        1000, 1250, 1000, 12500, 1250, 1250, 12500, 1000, 12500, 1250, 1250, 12500, 1250, 1250, 1000, 1000]
H1, H2 = 512, 256
P = 128
TB = B // P
NJ = F // 2
NBANK = 4
STRIPS = 4
COUPLE_GROUPS = 15
GROUPS = COUPLE_GROUPS + 1
CHUNK_GROUPS = 2
CHUNKS = GROUPS // CHUNK_GROUPS
GW = 4 * P
SW = 4 * E
LOOKUP_US = 4.15
FIRST_LOOKUP_US, LANDS_US = 3.0, 2.5
FIRST_HOT_US, HOT_US = 12.0, 8.0
TURN_US, GROUP_US = 1.0, 2.65
K_LO_US = 2.4
VECTOR_CHUNKS = 6
BANK_W = COUPLE_GROUPS * GW + SW


HOT_STAGES = 3
HOT_FIELDS = 2 * HOT_STAGES
HOT_ROWS, HOT_CHUNKS = 125, 8
HOT_VECTOR = 6


def field_order():
    small = [f for f in range(F) if ROWS[f] == HOT_ROWS * HOT_CHUNKS][:HOT_FIELDS]
    other = [f for f in range(F) if f not in small]
    order = []
    for J in range(NJ):
        order += [small.pop(0), small.pop(0)] if is_hot(J) else [other.pop(0), other.pop(0)]
    return order


def is_hot(J):
    return J % 2 == 0 and J < 2 * HOT_STAGES


def hot_index(J):
    return J // 2


def dma_index(J):
    return J - min((J + 1) // 2, HOT_STAGES)


def pair_index(i, j):
    return i * (2 * F - i - 1) // 2 + j - i - 1


def blocks():
    return [(m, J) for J in range(1, NJ) for m in range(J)]


def single_m(bank, strip):
    return STRIPS * bank + strip


def bank_pairs(bank):
    out = []
    for m, J in blocks()[2 * COUPLE_GROUPS * bank:2 * COUPLE_GROUPS * (bank + 1)]:
        for j in (2 * J, 2 * J + 1):
            out += [(2 * m, j), (2 * m + 1, j)]
    return out + [(2 * m, 2 * m + 1) for m in (single_m(bank, s) for s in range(STRIPS))]


def z_rows(bank):
    order = field_order()
    pairs = [pair_index(*sorted((order[i], order[j]))) for i, j in bank_pairs(bank)]
    row = np.zeros(P, np.int64)
    for c in range(STRIPS):
        for r in range(COUPLE_GROUPS):
            for h in range(2):
                row[32 * c + 2 * r + h] = pairs[8 * r + 2 * c + h]
        row[32 * c + 30] = pairs[8 * COUPLE_GROUPS + c]
        row[32 * c + 31] = F * (F - 1) // 2 + STRIPS * bank + c
    return row


def build(nc, ids, tables, kern, dense, w1, b1, w2, b2, w3, sel, place, ident_d, fold_d,
          hot_ids_d, hot_rows_d, out):
    F32, F32R, I32 = mybir.dt.float32, mybir.dt.float32r, mybir.dt.int32
    ALU, ACT = mybir.AluOpType, mybir.ActivationFunctionType
    XG, XS, KR, KS, TS = 4, 2, 3, 3, 2
    BLOCKS = blocks()

    ctx = ExitStack()
    with ctx:
        def sb(name, shape, dt=F32):
            return ctx.enter_context(nc.sbuf_tensor(name, shape, dt))

        def sem(name):
            return ctx.enter_context(nc.semaphore(name))

        ids_sb = sb("ids_sb", [P, TB, F], I32)
        gathered = sb("gathered", [P, XG, TB, 2 * E])
        split = sb("split", [P, XS, TB, 2, 2 * E], F32R)
        moving = sb("moving", [P, F, B], F32R)
        factor = sb("factor", [P, NJ, B])
        k_raw = sb("k_raw", [P, KR, CHUNK_GROUPS * GW])
        h1_sb = k_raw[:, 0:2, :].rearrange("p s (m b) -> p (s m) b", b=B)
        h2_sb = k_raw[:, 2, :].rearrange("p (m b) -> p m b", b=B)
        k_hi = sb("k_hi", [P, KS, CHUNK_GROUPS * GW], F32R)
        k_lo = sb("k_lo", [P, KS, CHUNK_GROUPS * GW], F32R)
        prod = sb("prod", [P, TS, 4, B])
        z_sb = sb("z_sb", [P, NBANK, B])
        y_sb = sb("y_sb", [1, B])
        w1_sb = sb("w1_sb", [P, NBANK, H1])
        w2_sb = sb("w2_sb", [P, H1 // P, H2])
        w3_sb = sb("w3_sb", [P, H2 // P])
        b1_sb = sb("b1_sb", [P, H1 // P])
        b2_sb = sb("b2_sb", [P, H2 // P])
        dense_sb = sb("dense_sb", [STRIPS, NBANK, B])
        place_sb = sb("place_sb", [STRIPS, P])
        sel_sb = sb("sel_sb", [P, 2, 62])
        ident = sb("ident", [P, P])
        fold = sb("fold", [P, 3 * E])
        fold_r = sb("fold_r", [P, 3 * E], F32R)
        hot_rows = sb("hot_rows", [HOT_ROWS, 2, HOT_CHUNKS])
        ident_r = sb("ident_r", [P, P], F32R)
        first_hot, first_table, first_ids = F - 2 * HOT_CHUNKS, F - 2 * HOT_CHUNKS - 4, NJ - HOT_FIELDS
        hot = moving[0:HOT_ROWS, first_hot:F, :].rearrange("p (s c) b -> p s c b", s=2)
        t_split = moving[0:HOT_ROWS, first_table:first_hot, :].rearrange("p (s q) n -> p s (q n)", s=2).rearrange(
            "p s (c e) -> p s c e", c=HOT_CHUNKS)
        hot_ids = factor[0:HOT_ROWS, first_ids:NJ, :].bitcast(I32)
        t_raw = z_sb[0:HOT_ROWS, :, :].rearrange("p s (c e) -> p s c e", e=E)
        far = w1_sb[0:HOT_ROWS, 0:HOT_CHUNKS - HOT_VECTOR, :]

        u_ps = [ctx.enter_context(nc.psum_tensor(f"u_ps{i}", [P, 2, B], F32)) for i in range(2)]
        z_ps = [ctx.enter_context(nc.psum_tensor(f"z_ps{i}", [P, B], F32)) for i in range(2)]
        t_ps = [ctx.enter_context(nc.psum_tensor(f"t_ps{i}", [P, B], F32)) for i in range(2)]

        ids_in = sem("ids_in")
        const_in = sem("const_in")
        weights_in = sem("weights_in")
        field_in = [sem(f"field_in{J}") for J in range(NJ)]
        k_in = [sem(f"k_in{i}") for i in range(KR)]
        hot_ids_in = [sem(f"hot_ids_in{i}") for i in range(HOT_STAGES)]
        hot_rows_in = sem("hot_rows_in")
        t_in = [sem(f"t_in{i}") for i in range(NBANK)]
        t_hi_ready = sem("t_hi_ready")
        t_lo_ready = sem("t_lo_ready")
        hot_vector = sem("hot_vector")
        hot_scalar = sem("hot_scalar")
        far_ready = sem("far_ready")
        ident_ready = sem("ident_ready")
        k_hi_ready = sem("k_hi_ready")
        k_lo_ready = sem("k_lo_ready")
        k_lo_late = sem("k_lo_late")
        x_hi_ready = sem("x_hi_ready")
        x_lo_ready = sem("x_lo_ready")
        turned = sem("turned")
        x_ready = sem("x_ready")
        u_ready = sem("u_ready")
        prod_ready = sem("prod_ready")
        summed = sem("summed")
        z_ready = sem("z_ready")
        h1_done = sem("h1_done")
        h1_ready = sem("h1_ready")
        h2_done = sem("h2_done")
        h2_ready = sem("h2_ready")
        y_done = sem("y_done")
        y_ready = sem("y_ready")
        y_out = sem("y_out")

        NG = NBANK * GROUPS

        def group_blocks(g):
            k, r = divmod(g, GROUPS)
            if r < COUPLE_GROUPS:
                two = BLOCKS[2 * (COUPLE_GROUPS * k + r):][:2]
                return [(m, (2 * J, 2 * J + 1)) for m, J in two]
            return [(single_m(k, s), (2 * single_m(k, s) + 1, 2 * single_m(k, s) + 3)) for s in (0, 2)]

        def last_stage(g):
            return max(j // 2 for _, js in group_blocks(g) for j in js)

        def last_factor(g):
            return max(m for m, _ in group_blocks(g)) + (g % GROUPS == COUPLE_GROUPS)

        pool_steps, pool_now = [], FIRST_LOOKUP_US
        arrives = {J: FIRST_HOT_US + HOT_US * hot_index(J) for J in range(NJ) if is_hot(J)}
        lookups = [(J, h) for J in range(NJ) if not is_hot(J) for h in range(2)]

        def look_up(J):
            turns = [("turn", 3 * J + q) for q in range(3)]
            if not is_hot(J):
                return [[("split", J)], turns[:2], turns[2:]]
            h = 2 * hot_index(J)
            again = [[("hot", q), ("table", q)] if q < HOT_FIELDS else [] for q in (h + 2, h + 3)]
            return [[turns[0]] + again[0], [turns[1]] + again[1], turns[2:]]

        steps = [("hot", 0), ("table", 0), ("hot", 1), ("table", 1), ("chunk", 0)]
        staged, now, doing = -1, 0, []
        for g in range(NG):
            while lookups and (pool_now <= now or lookups[0][0] <= last_stage(g)):
                J, h = lookups.pop(0)
                pool_steps.append(("lookup", J, h))
                pool_now += LOOKUP_US
                arrives[J] = pool_now + LANDS_US
            while True:
                if doing:
                    urgent = (staged < last_stage(g) or staged == last_stage(g) and len(doing) > 1
                              or staged <= last_factor(g))
                    steps += doing.pop(0)
                    if not urgent:
                        break
                elif staged < last_stage(g) or arrives.get(staged + 1, now + 1) <= now:
                    staged += 1
                    now = max(now, arrives[staged]) + TURN_US
                    doing = look_up(staged)
                else:
                    break
            if g % CHUNK_GROUPS == 0 and g // CHUNK_GROUPS + 1 < NG // CHUNK_GROUPS:
                n = g // CHUNK_GROUPS + 1
                steps.append(("chunk", n))
                if n >= VECTOR_CHUNKS:
                    pool_steps.append(("chunk", n, 0))
                    pool_now = max(pool_now, now) + K_LO_US
            steps.append(("group", g))
            now += GROUP_US
            if g:
                steps.append(("sum", g - 1))
                if g % GROUPS == 0:
                    steps.append(("bank", g // GROUPS - 1))
        steps += [("sum", NG - 1), ("bank", NBANK - 1)]

        def chunk_width(n):
            return CHUNK_GROUPS * GW if (n + 1) % CHUNKS else (CHUNK_GROUPS - 1) * GW + SW

        def columns(g):
            return (g % CHUNK_GROUPS) * GW, (P if g % GROUPS < COUPLE_GROUPS else E)

        def h1_ps(m):
            return (t_ps[0][:, :], t_ps[1][:, :], z_ps[0][:, :], u_ps[0][:, 0, :])[m]

        def wait_k_lo(eng, n):
            if n < VECTOR_CHUNKS:
                eng.wait_ge(k_lo_ready, n + 1)
            else:
                eng.wait_ge(k_lo_late, n - VECTOR_CHUNKS + 1)

        def wait_hot_turned(eng, h):
            eng.wait_ge(turned, 3 * 2 * (h // 2) + h % 2 + 1)

        def wait_dma_turned(eng, d):
            J = next(J for J in range(NJ) if not is_hot(J) and dma_index(J) == d)
            eng.wait_ge(turned, 3 * J + 2)

        order = field_order()
        block = ctx.enter_context(nc.Block())

        @block.sync
        def _(sp):
            def load_table(h):
                sp.dma_start(t_raw[:, h % NBANK, :, :],
                             tables[order[4 * (h // 2) + h % 2]].rearrange("(p c) e -> p c e", c=HOT_CHUNKS)
                             ).then_inc(t_in[h % NBANK], 16)

            def load_hot_ids(i):
                sp.dma_start(hot_ids[:, 2 * i:2 * i + 2, :],
                             hot_ids_d[:, 2 * i:2 * i + 2, :].to_broadcast([HOT_ROWS, 2, B])).then_inc(hot_ids_in[i], 16)

            def load_chunk(n):
                at = (n // CHUNKS) * BANK_W + (n % CHUNKS) * CHUNK_GROUPS * GW
                if n >= KR:
                    wait_k_lo(sp, n - KR)
                for half in range(2):
                    sp.dma_start(k_raw[half * E:(half + 1) * E, n % KR, 0:chunk_width(n)],
                                 kern[:, at:at + chunk_width(n)]).then_inc(k_in[n % KR], 16)

            sp.dma_start(ids_sb[:, :, :], ids).then_inc(ids_in, 16)
            sp.dma_start(hot_rows[:, :, :], hot_rows_d).then_inc(hot_rows_in, 16)
            load_hot_ids(0)
            load_table(0)
            load_table(1)
            load_chunk(0)
            for i in range(1, HOT_STAGES):
                load_hot_ids(i)
                if 2 * i < NBANK:
                    load_table(2 * i)
                    load_table(2 * i + 1)
                if i < KR:
                    load_chunk(i)
            for n in range(min(HOT_STAGES, KR), KR):
                load_chunk(n)
            for h in range(NBANK, HOT_FIELDS):
                sp.wait_ge(t_lo_ready, h - NBANK + 1)
                load_table(h)
            for n in range(KR, NBANK * CHUNKS):
                load_chunk(n)
                if n == 10:
                    sp.wait_ge(turned, 3 * (2 * HOT_STAGES - 1))
                    sp.dma_start(w1_sb[:, :, :], w1).then_inc(weights_in, 16)
                    sp.dma_start(w2_sb[:, :, :], w2).then_inc(weights_in, 16)
                    sp.dma_start(w3_sb[:, :], w3).then_inc(weights_in, 16)
                    sp.dma_start(b1_sb[:, :], b1).then_inc(weights_in, 16)
                    sp.dma_start(b2_sb[:, :], b2).then_inc(weights_in, 16)
            sp.wait_ge(y_ready, 1)
            sp.dma_start(out, y_sb[:, :]).then_inc(y_out, 16)
            sp.wait_ge(y_out, 16)

        @block.gpsimd
        def _(pool):
            pool.wait_ge(ids_in, 16)
            for what, n, h in pool_steps:
                if what == "lookup":
                    d = dma_index(n)
                    if d >= XG:
                        pool.wait_ge(x_lo_ready, d - XG + 1)
                    for t in range(TB):
                        f = order[2 * n + h]
                        pool.indirect_dma_start(
                            gathered[:, d % XG, t, h * E:(h + 1) * E], None, tables[f],
                            bass.IndirectOffsetOnAxis(ap=ids_sb[:, t, f:f + 1], axis=0),
                        ).then_inc(field_in[n], 16)
                elif what == "chunk":
                    w = chunk_width(n)
                    pool.wait_ge(k_hi_ready, n + 1)
                    pool.tensor_tensor(k_lo[:, n % KS, 0:w], k_raw[:, n % KR, 0:w],
                                       k_hi[:, n % KS, 0:w].bitcast(F32), ALU.subtract).then_inc(k_lo_late, 1)

        @block.scalar
        def _(act):
            act.dma_start(ident[:, :], ident_d).then_inc(const_in, 16)
            act.dma_start(fold[:, :], fold_d).then_inc(const_in, 16)
            act.dma_start(sel_sb[:, :, :], sel).then_inc(const_in, 16)
            act.dma_start(place_sb[:, :], place).then_inc(const_in, 16)
            act.dma_start(dense_sb[:, :, :], dense).then_inc(const_in, 16)
            act.wait_ge(const_in, 5 * 16)
            act.copy(ident_r[:, :], ident[:, :]).then_inc(ident_ready, 1)
            act.copy(fold_r[:, :], fold[:, :]).then_inc(ident_ready, 1)
            n_far = 0
            for what, n in steps:
                if what == "chunk":
                    w = chunk_width(n)
                    act.wait_ge(k_in[n % KR], 32 * (n // KR + 1))
                    if n >= KS:
                        act.wait_ge(u_ready, 2 * CHUNK_GROUPS * (n - KS + 1))
                    act.copy(k_hi[:, n % KS, 0:w], k_raw[:, n % KR, 0:w]).then_inc(k_hi_ready, 1)
                elif what == "table":
                    act.wait_ge(t_in[n % NBANK], 16 * (n // NBANK + 1))
                    if n >= 2:
                        wait_hot_turned(act, n - 2)
                    act.copy(t_split[:, n % 2, :, 0:E], t_raw[:, n % NBANK, :, :]).then_inc(t_hi_ready, 1)
                elif what == "hot":
                    act.wait_ge(hot_rows_in, 16)
                    act.wait_ge(hot_ids_in[n // 2], 16)
                    for c in range(HOT_VECTOR, HOT_CHUNKS):
                        if n:
                            act.wait_ge(hot_scalar, n)
                        act.activation(far[:, c - HOT_VECTOR, :], hot_ids[:, n, :], ACT.Abs,
                                       bias=hot_rows[:, 1, c:c + 1]).then_inc(far_ready, 1)
                        n_far += 1
                    act.wait_ge(far_ready, n_far)
                    if n >= 2:
                        wait_hot_turned(act, n - 2)
                    act.activation(hot[:, n % 2, HOT_VECTOR:, :], far, ACT.Relu,
                                   scale=-1.0, bias=1.0).then_inc(hot_scalar, 1)
                elif what == "split":
                    d = dma_index(n)
                    act.wait_ge(field_in[n], 2 * TB * 16)
                    if d >= XS:
                        wait_dma_turned(act, d - XS)
                    act.copy(split[:, d % XS, :, :, 0:E],
                             gathered[:, d % XG, :, :].rearrange("p t (h e) -> p t h e", h=2)).then_inc(x_hi_ready, 1)
                elif what == "turn":
                    J, q = divmod(n, 3)
                    act.wait_ge(turned, n + 1)
                    to = moving[:, 2 * J + q, :] if q < 2 else factor[:, J, :]
                    act.copy(to, t_ps[n % 2][:, :]).then_inc(x_ready, 1)
                elif what == "bank":
                    act.wait_ge(summed, GROUPS * (n + 1))
                    act.copy(z_sb[:, n, :], z_ps[n % 2][:, :]).then_inc(z_ready, 1)
            act.wait_ge(weights_in, 5 * 16)
            for m in range(H1 // P):
                act.wait_ge(h1_done, m + 1)
                act.activation(h1_sb[:, m, :], h1_ps(m), ACT.Relu, bias=b1_sb[:, m:m + 1]).then_inc(h1_ready, 1)
            for m in range(H2 // P):
                act.wait_ge(h2_done, m + 1)
                act.activation(h2_sb[:, m, :], u_ps[1][:, m, :], ACT.Relu, bias=b2_sb[:, m:m + 1]).then_inc(h2_ready, 1)
            act.wait_ge(y_done, 1)
            act.copy(y_sb[:, :], t_ps[0][0:1, :]).then_inc(y_ready, 1)

        @block.vector
        def _(dve):
            for what, n in steps:
                if what == "chunk" and n < VECTOR_CHUNKS:
                    w = chunk_width(n)
                    dve.wait_ge(k_hi_ready, n + 1)
                    dve.tensor_tensor(k_lo[:, n % KS, 0:w], k_raw[:, n % KR, 0:w],
                                      k_hi[:, n % KS, 0:w].bitcast(F32), ALU.subtract).then_inc(k_lo_ready, 1)
                elif what == "table":
                    dve.wait_ge(t_hi_ready, n + 1)
                    dve.tensor_tensor(t_split[:, n % 2, :, E:2 * E], t_raw[:, n % NBANK, :, :],
                                      t_split[:, n % 2, :, 0:E].bitcast(F32), ALU.subtract).then_inc(t_lo_ready, 1)
                elif what == "hot":
                    dve.wait_ge(hot_rows_in, 16)
                    dve.wait_ge(hot_ids_in[n // 2], 16)
                    if n >= 2:
                        wait_hot_turned(dve, n - 2)
                    for c in range(HOT_VECTOR):
                        last = dve.tensor_scalar(hot[:, n % 2, c, :], hot_ids[:, n, :], hot_rows[:, 0, c:c + 1], None,
                                                 ALU.is_equal)
                    last.then_inc(hot_vector, 1)
                elif what == "split":
                    d = dma_index(n)
                    dve.wait_ge(x_hi_ready, d + 1)
                    dve.tensor_tensor(split[:, d % XS, :, :, E:2 * E],
                                      gathered[:, d % XG, :, :].rearrange("p t (h e) -> p t h e", h=2),
                                      split[:, d % XS, :, :, 0:E].bitcast(F32), ALU.subtract).then_inc(x_lo_ready, 1)
                elif what == "group":
                    rows = P if n % GROUPS < COUPLE_GROUPS else E
                    for h, (m, js) in enumerate(group_blocks(n)):
                        bl = 2 * n + h
                        dve.wait_ge(u_ready, bl + 1)
                        dve.wait_ge(x_ready, 3 * (last_factor(n) + 1))
                        if n >= TS:
                            dve.wait_ge(summed, n - TS + 1)
                        if rows == P:
                            by = factor[:, m:m + 1, :].to_broadcast([P, 2, B])
                        else:
                            by = factor[0:rows, m:m + 2, :]
                        dve.tensor_tensor(prod[0:rows, n % TS, 2 * h:2 * h + 2, :], u_ps[bl % 2][0:rows, :, :],
                                          by, ALU.mult).then_inc(prod_ready, 1)

        @block.tensor
        def _(pe):
            pe.wait_ge(ident_ready, 2)
            for what, n in steps:
                if what == "turn":
                    J, q = divmod(n, 3)
                    if n >= 2:
                        pe.wait_ge(x_ready, n - 1)
                    to = t_ps[n % 2]
                    if q == 2:
                        pe.wait_ge(x_ready, n)
                        pe.matmul(to[:, :], fold_r[:, E:3 * E], moving[:, 2 * J, :], start=True, stop=False)
                        last = pe.matmul(to[:, :], fold_r[:, 0:2 * E], moving[:, 2 * J + 1, :], start=False, stop=True)
                    elif is_hot(J):
                        h = 2 * hot_index(J) + q
                        pe.wait_ge(t_lo_ready, h + 1)
                        pe.wait_ge(hot_vector, h + 1)
                        pe.wait_ge(hot_scalar, h + 1)
                        for c in range(HOT_CHUNKS):
                            last = pe.matmul(to[:, :], t_split[:, h % 2, c, :], hot[:, h % 2, c, :],
                                             start=c == 0, stop=c == HOT_CHUNKS - 1)
                    else:
                        pe.wait_ge(x_lo_ready, dma_index(J) + 1)
                        for t in range(TB):
                            last = pe.transpose(to[:, t * P:(t + 1) * P].bitcast(F32R),
                                                split[:, dma_index(J) % XS, t, q, :], ident_r[:, :])
                    last.then_inc(turned, 1)
                elif what == "group":
                    k, r = divmod(n, GROUPS)
                    slot = n // CHUNK_GROUPS % KS
                    first, width = columns(n)
                    wait_k_lo(pe, n // CHUNK_GROUPS)
                    pe.wait_ge(x_ready, 3 * last_stage(n) + 2)
                    if r == 0:
                        if k >= 2:
                            pe.wait_ge(z_ready, k - 1)
                        pe.matmul(z_ps[k % 2][:, :], place_sb[:, :], dense_sb[:, k, :], start=True, stop=False)
                    for h, (m, js) in enumerate(group_blocks(n)):
                        bl = 2 * n + h
                        if bl >= 2:
                            pe.wait_ge(prod_ready, bl - 1)
                        for c, j in enumerate(js):
                            at = first + (2 * h + c) * width
                            pe.matmul(u_ps[bl % 2][0:width, c, :], k_hi[:, slot, at:at + width], moving[:, j, :],
                                      start=True, stop=False)
                            last = pe.matmul(u_ps[bl % 2][0:width, c, :], k_lo[:, slot, at:at + width], moving[:, j, :],
                                             start=False, stop=True)
                        last.then_inc(u_ready, 1)
                elif what == "sum":
                    k, r = divmod(n, GROUPS)
                    single = r == COUPLE_GROUPS
                    rows = E if single else P
                    pe.wait_ge(prod_ready, 2 * n + 2)
                    if n == NG - 1:
                        pe.wait_ge(weights_in, 5 * 16)
                        pe.wait_ge(z_ready, NBANK - 1)
                        for m in range(H1 // P):
                            for kk in range(NBANK - 1):
                                pe.matmul(h1_ps(m), w1_sb[:, kk, m * P:(m + 1) * P], z_sb[:, kk, :],
                                          start=kk == 0, stop=False)
                    for c in range(STRIPS):
                        s = sel_sb[0:rows, 1, 1:33] if single else sel_sb[0:rows, 0, 30 - 2 * r:62 - 2 * r]
                        last = pe.matmul(z_ps[k % 2][32 * c:32 * c + 32, :], s, prod[0:rows, n % TS, c, :],
                                         start=False, stop=single)
                    last.then_inc(summed, 1)
            pe.wait_ge(z_ready, NBANK)
            for m in range(H1 // P):
                pe.matmul(h1_ps(m), w1_sb[:, NBANK - 1, m * P:(m + 1) * P], z_sb[:, NBANK - 1, :],
                          start=False, stop=True).then_inc(h1_done, 1)
            for m in range(H2 // P):
                for kk in range(H1 // P):
                    pe.wait_ge(h1_ready, kk + 1)
                    last = pe.matmul(u_ps[1][:, m, :], w2_sb[:, kk, m * P:(m + 1) * P], h1_sb[:, kk, :],
                                     start=kk == 0, stop=kk == H1 // P - 1)
                last.then_inc(h2_done, 1)
            for kk in range(H2 // P):
                pe.wait_ge(h2_ready, kk + 1)
                last = pe.matmul(t_ps[0][0:1, :], w3_sb[:, kk:kk + 1], h2_sb[:, kk, :],
                                 start=kk == 0, stop=kk == H2 // P - 1)
            last.then_inc(y_done, 1)


def kernel(**inputs):
    import concourse.bacc as _bacc
    from concourse.bass_utils import run_bass_kernel_spmd as _run

    a = {k: np.asarray(v) for k, v in inputs.items()}
    order = field_order()
    kt = np.empty((E, NBANK * BANK_W // E, E), np.float32)
    for n, (i, j) in enumerate(pair for k in range(NBANK) for pair in bank_pairs(k)):
        i, j = order[i], order[j]
        one = a["L0_rec_kernel"][:, pair_index(*sorted((i, j))), :]
        kt[:, n, :] = one if i < j else one.T
    kt = kt.reshape(E, NBANK * BANK_W)
    rows = np.concatenate([z_rows(k) for k in range(NBANK)])

    sel = np.zeros((P, 2, 62), np.float32)
    sel[:E, 0, 30] = 1
    sel[E:, 0, 31] = 1
    sel[:E, 1, 31] = 1
    place = np.zeros((STRIPS, P), np.float32)
    for c in range(STRIPS):
        place[c, 32 * c + 31] = 1

    fold = np.zeros((P, 3 * E), np.float32)
    fold[:, E:2 * E] = np.tile(np.eye(E), (2, 1))
    hot_rows = (HOT_CHUNKS * np.arange(HOT_ROWS)[:, None] + np.arange(HOT_CHUNKS)).astype(np.float32)
    hot_fields = [order[2 * J + h] for J in range(NJ) if is_hot(J) for h in range(2)]

    arrays = {
        "fold": fold, "hot_rows": np.stack([hot_rows, -hot_rows], 1),
        "hot_ids": a["ids"][:, hot_fields].T[None],
        "ids": a["ids"].reshape(TB, P, F).transpose(1, 0, 2),
        **{f"tbl_{f}": a[f"tbl_{f}"] for f in range(F)},
        "kern": kt,
        "dense": a["dense_ctx"].T.reshape(NBANK, STRIPS, B).transpose(1, 0, 2),
        "w1": a["W_top1"][rows].reshape(NBANK, P, H1).transpose(1, 0, 2),
        "b1": a["b_top1"].reshape(H1 // P, P).T,
        "w2": a["W_top2"].reshape(H1 // P, P, H2).transpose(1, 0, 2),
        "b2": a["b_top2"].reshape(H2 // P, P).T,
        "w3": a["W_top3"].reshape(H2 // P, P).T,
        "sel": sel, "place": place, "ident": np.eye(P, dtype=np.float32),
    }
    arrays = {f"in_{k}": np.ascontiguousarray(v) for k, v in arrays.items()}
    nc = _bacc.Bacc("TRN2", target_bir_lowering=False, num_devices=1)
    ap = {k: nc.dram_tensor(k, v.shape, mybir.dt.from_np(v.dtype), kind="ExternalInput").ap() for k, v in arrays.items()}
    out = nc.dram_tensor("out_y", (1, B), mybir.dt.float32, kind="ExternalOutput").ap()
    build(nc, ap["in_ids"], [ap[f"in_tbl_{f}"] for f in range(F)], ap["in_kern"], ap["in_dense"], ap["in_w1"],
          ap["in_b1"], ap["in_w2"], ap["in_b2"], ap["in_w3"], ap["in_sel"], ap["in_place"], ap["in_ident"], ap["in_fold"],
          ap["in_hot_ids"], ap["in_hot_rows"], out)
    r = _run(nc, [arrays], core_ids=[0])
    return r.results[0]["out_y"].reshape(B, 1)
```

```python
from contextlib import ExitStack

import numpy as np

import concourse.bass as bass
from concourse import mybir

B, F, E = 512, 32, 64
ROWS = [1000, 125000, 1250, 12500, 12500, 1250, 125000, 1250, 1000, 1000, 1000, 125000, 12500, 1250, 1250, 1000,
        1000, 1250, 1000, 12500, 1250, 1250, 12500, 1000, 12500, 1250, 1250, 12500, 1250, 1250, 1000, 1000]
H1, H2 = 512, 256
P = 128
TB = B // P
NJ = F // 2
NBANK = 4
STRIPS = 4
COUPLE_GROUPS = 15
GROUPS = COUPLE_GROUPS + 1
CHUNK_GROUPS = 2
CHUNKS = GROUPS // CHUNK_GROUPS
GW = 4 * P
SW = 4 * E
BANK_W = COUPLE_GROUPS * GW + SW
NG = NBANK * GROUPS
XG, XS, KR, KS, TS = 4, 2, 3, 3, 2

HOT_STAGES = 2
HOT_FIELDS = 2 * HOT_STAGES
HOT_ROWS, HOT_CHUNKS = 125, 8

LOOKUP_US = 4.15
LANDS_US = 1.8
POOL_K_LO_US = 2.5
LOAD_US = 3.6
COPY_US = 0.5
K_HI_US = 0.96
K_LO_US = 1.15
SPLIT_LO_US = 0.6
PRODUCT_US = 1.135
BLOCK_US = 0.88
SUM_US = 0.9
FACTOR_US = 0.45
TURN_US = 0.25
HOP_US = 0.2
FIRST_LOOKUP_US = 2.8
OPENED_US = 27.0
FIRST_WARM = 24
SLACK_US = 0.3
TURN_SLACK_US = 0.6
CHUNK_AHEAD, TURN_AHEAD, SPLIT_AHEAD = 3, 3, 5
VECTOR_CHUNKS = 6
WEIGHTS_AFTER = 10


assert HOT_STAGES == 2


def field_order():
    small = [f for f in range(F) if ROWS[f] == HOT_ROWS * HOT_CHUNKS][:HOT_FIELDS]
    other = [f for f in range(F) if f not in small]
    order = []
    for J in range(NJ):
        order += [small.pop(0), small.pop(0)] if is_hot(J) else [other.pop(0), other.pop(0)]
    return order


def is_hot(J):
    return J % 2 == 0 and J < 2 * HOT_STAGES


def hot_index(J):
    return J // 2


def dma_index(J):
    return J - min((J + 1) // 2, HOT_STAGES)


def pair_index(i, j):
    return i * (2 * F - i - 1) // 2 + j - i - 1


def blocks():
    return [(m, J) for J in range(1, NJ) for m in range(J)]


def single_m(bank, strip):
    return STRIPS * bank + strip


def bank_pairs(bank):
    out = []
    for m, J in blocks()[2 * COUPLE_GROUPS * bank:2 * COUPLE_GROUPS * (bank + 1)]:
        for j in (2 * J, 2 * J + 1):
            out += [(2 * m, j), (2 * m + 1, j)]
    return out + [(2 * m, 2 * m + 1) for m in (single_m(bank, s) for s in range(STRIPS))]


def z_rows(bank):
    order = field_order()
    pairs = [pair_index(*sorted((order[i], order[j]))) for i, j in bank_pairs(bank)]
    row = np.zeros(P, np.int64)
    for c in range(STRIPS):
        for r in range(COUPLE_GROUPS):
            for h in range(2):
                row[32 * c + 2 * r + h] = pairs[8 * r + 2 * c + h]
        row[32 * c + 30] = pairs[8 * COUPLE_GROUPS + c]
        row[32 * c + 31] = F * (F - 1) // 2 + STRIPS * bank + c
    return row


def group_blocks(g):
    k, r = divmod(g, GROUPS)
    if r < COUPLE_GROUPS:
        return [(m, (2 * J, 2 * J + 1)) for m, J in blocks()[2 * (COUPLE_GROUPS * k + r):][:2]]
    return [(single_m(k, s), (2 * single_m(k, s) + 1, 2 * single_m(k, s) + 3)) for s in (0, 2)]


def last_stage(g):
    return max(j // 2 for _, js in group_blocks(g) for j in js)


def last_factor(g):
    return max(m for m, _ in group_blocks(g)) + (g % GROUPS == COUPLE_GROUPS)


def plan():
    first_group = [min(g for g in range(NG) if last_stage(g) >= J) for J in range(NJ)]
    dma_stages = [J for J in range(NJ) if not is_hot(J)]
    never = float("inf")

    steps = [("hot", 0), ("table", 0), ("hot", 1), ("table", 1), ("warm", FIRST_WARM), ("turn", 0),
             ("hot", 2), ("turn", 1), ("split", 1), ("table", 2), ("hot", 3), ("turn", 2), ("table", 3),
             ("turn", 3), ("turn", 4), ("chunk", 0), ("turn", 6), ("turn", 5), ("split", 3), ("chunk", 1),
             ("turn", 7), ("turn", 9), ("group", 0), ("turn", 10), ("turn", 8)]
    pool_steps = []
    lookups = [(J, h) for J in dma_stages for h in range(2)]
    pool_chunks = []

    free = {"pe": OPENED_US, "act": OPENED_US, "dve": OPENED_US + 1, "pool": FIRST_LOOKUP_US}
    landed = {}
    x_low = {J: OPENED_US for what, J in steps if what == "split"}
    turned = {n: OPENED_US for n in range(11)}
    k_high = {0: OPENED_US, 1: OPENED_US}
    k_low = dict(k_high)
    block, product = {0: OPENED_US, 1: OPENED_US}, {0: OPENED_US, 1: OPENED_US + 1}
    summed = {}

    def run(engine, ready, time):
        free[engine] = max(free[engine], ready) + time
        return free[engine] + HOP_US

    def place_free():
        d = dma_index(lookups[0][0])
        return 0 if d < XG else x_low.get(dma_stages[d - XG], never)

    def pool_lookup():
        J, h = lookups[0]
        done = run("pool", place_free(), LOOKUP_US)
        lookups.pop(0)
        pool_steps.append(("lookup", J, h))
        if h == 1:
            landed[J] = done + LANDS_US

    def pool_chunk():
        n = pool_chunks.pop(0)
        pool_steps.append(("chunk", n, 0))
        k_low[n] = run("pool", k_high[n], POOL_K_LO_US)

    def pool_until(time):
        while free["pool"] < time:
            chunk = max(free["pool"], k_high[pool_chunks[0]]) if pool_chunks else never
            lookup = max(free["pool"], place_free()) if lookups else never
            if min(chunk, lookup) >= time:
                break
            pool_chunk() if chunk <= lookup else pool_lookup()

    def chunk_loaded(n):
        loaded = k_low.get(n - KR, never) + LOAD_US if n >= KR else 0
        return max(loaded, block.get(2 * CHUNK_GROUPS * (n - KS + 1) - 1, 0))

    def add_chunk(n):
        if n >= KR and n - KR not in k_low:
            pool_chunk()
        steps.append(("chunk", n))
        k_high[n] = run("act", chunk_loaded(n), K_HI_US)
        if n < VECTOR_CHUNKS:
            k_low[n] = run("dve", k_high[n], K_LO_US)
        else:
            pool_chunks.append(n)

    def add_split(J):
        while J not in landed:
            pool_lookup()
        steps.append(("split", J))
        x_low[J] = run("dve", run("act", landed[J], COPY_US), SPLIT_LO_US)

    def turn_ready(n):
        return x_low.get(n // 3, never) if n % 3 < 2 else turned[n - 1]

    def add_turn(n):
        if n // 3 not in x_low:
            add_split(n // 3)
        steps.append(("turn", n))
        ready = max(turned[n - 2], turn_ready(n))
        turned[n] = run("act", run("pe", ready, TURN_US if n % 3 < 2 else FACTOR_US), COPY_US)

    for g in range(1, NG):
        while len(turned) <= max(3 * last_stage(g) + 1, 3 * last_factor(g) + 2):
            add_turn(len(turned))
        while g // CHUNK_GROUPS not in k_high:
            add_chunk(len(k_high))
        pool_until(free["pe"])
        n = len(turned)
        while (n < 3 * NJ and first_group[n // 3] <= g + TURN_AHEAD
               and turn_ready(n) <= max(free["pe"], product[2 * g - 2]) + TURN_SLACK_US):
            add_turn(n)
            n += 1
        n = len(k_high)
        if n < NG // CHUNK_GROUPS and n <= (g + CHUNK_AHEAD) // CHUNK_GROUPS:
            begin = chunk_loaded(n) if n >= VECTOR_CHUNKS else max(chunk_loaded(n), free["act"])
            if begin <= max(free["act"] if n >= VECTOR_CHUNKS else 0, free["dve"] - K_HI_US) + SLACK_US:
                add_chunk(n)
        J = next((J for J in dma_stages if J not in x_low), None)
        if (J is not None and first_group[J] <= g + SPLIT_AHEAD and dma_index(J) < XS + dma_index(len(turned) // 3)
                and max(landed.get(J, never), free["act"]) + COPY_US <= free["dve"] + SLACK_US):
            add_split(J)
        while g // CHUNK_GROUPS not in k_low:
            pool_chunk()

        steps.append(("group", g))
        for bl in (2 * g, 2 * g + 1):
            ready = max(k_low[g // CHUNK_GROUPS], turned[3 * last_stage(g) + 1], product[bl - 2])
            block[bl] = run("pe", ready, BLOCK_US)
            ready = max(block[bl], turned[3 * last_factor(g) + 2], summed.get(g - TS, 0))
            product[bl] = run("dve", ready, PRODUCT_US)
        steps.append(("sum", g - 1))
        summed[g - 1] = run("pe", product[2 * g - 1], SUM_US)
        if (g - 1 + TS) % GROUPS == COUPLE_GROUPS:
            steps.append(("dense", g // GROUPS))
        if g % GROUPS == 0:
            steps.append(("bank", g // GROUPS - 1))
            run("act", summed[g - 1], COPY_US)
    return steps + [("sum", NG - 1), ("bank", NBANK - 1)], pool_steps


def build(nc, ids, tables, kern, dense, w1, b1, w2, b2, w3, sel, ident_d, fold_d,
          hot_ids_d, hot_rows_d, out):
    F32, F32R, I32 = mybir.dt.float32, mybir.dt.float32r, mybir.dt.int32
    ALU, ACT = mybir.AluOpType, mybir.ActivationFunctionType

    ctx = ExitStack()
    with ctx:
        def sb(name, shape, dt=F32):
            return ctx.enter_context(nc.sbuf_tensor(name, shape, dt))

        def sem(name):
            return ctx.enter_context(nc.semaphore(name))

        ids_sb = sb("ids_sb", [P, TB, F], I32)
        gathered = sb("gathered", [P, XG, TB, 2 * E])
        split = sb("split", [P, XS, TB, 2, 2 * E], F32R)
        moving = sb("moving", [P, F, B], F32R)
        factor = sb("factor", [P, NJ, B])
        k_raw = sb("k_raw", [P, KR, CHUNK_GROUPS * GW])
        h1_sb = k_raw[:, 0:2, :].rearrange("p s (m b) -> p (s m) b", b=B)
        h2_sb = k_raw[:, 2, :].rearrange("p (m b) -> p m b", b=B)
        k_hi = sb("k_hi", [P, KS, CHUNK_GROUPS * GW], F32R)
        k_lo = sb("k_lo", [P, KS, CHUNK_GROUPS * GW], F32R)
        prod = sb("prod", [P, TS, 4, B])
        z_sb = sb("z_sb", [P, NBANK, B])
        y_sb = z_sb[0:1, 0, :]
        w1_sb = sb("w1_sb", [P, NBANK, H1])
        w2_sb = gathered[:, 0:XG // 2, :, :].rearrange("p s t e -> p (s t e)").rearrange("p (k n) -> p k n", n=H2)
        w3_sb = sb("w3_sb", [P, H2 // P])
        b1_sb = sb("b1_sb", [P, H1 // P])
        b2_sb = sb("b2_sb", [P, H2 // P])
        sel_sb = sb("sel_sb", [P, 2, 62])
        ident, fold = prod[:, 1, 0, 0:P], prod[:, 1, 1, 0:3 * E]
        fold_r = sb("fold_r", [P, 3 * E], F32R)
        zeros = sb("zeros", [P, B], mybir.dt.bfloat16)
        hot_rows = sb("hot_rows", [HOT_ROWS, HOT_CHUNKS])
        ident_r = sb("ident_r", [P, P], F32R)
        first_hot, first_table, first_ids = F - 2 * HOT_CHUNKS, F - 2 * HOT_CHUNKS - 4, NJ - HOT_FIELDS
        hot = [moving[0:HOT_ROWS, first_hot:F - HOT_CHUNKS, :], moving[0:HOT_ROWS, F - HOT_CHUNKS:F, :]]
        t_split = moving[0:HOT_ROWS, first_table:first_hot, :].rearrange("p (s q) n -> p s (q n)", s=2).rearrange(
            "p s (c e) -> p s c e", c=HOT_CHUNKS)
        hot_ids = factor[0:HOT_ROWS, first_ids:NJ, :].bitcast(I32)
        t_raw = z_sb[0:HOT_ROWS, :, :].rearrange("p s (c e) -> p s c e", e=E)

        u_ps = [ctx.enter_context(nc.psum_tensor(f"u_ps{i}", [P, 2, B], F32)) for i in range(2)]
        z_ps = [ctx.enter_context(nc.psum_tensor(f"z_ps{i}", [P, B], F32)) for i in range(2)]
        t_ps = [ctx.enter_context(nc.psum_tensor(f"t_ps{i}", [P, B], F32)) for i in range(2)]

        ids_in = sem("ids_in")
        const_in = sem("const_in")
        dense_in = sem("dense_in")
        weights_in = sem("weights_in")
        w2_in = sem("w2_in")
        field_in = [sem(f"field_in{J}") for J in range(NJ)]
        k_in = [sem(f"k_in{i}") for i in range(KR)]
        hot_ids_in = [sem(f"hot_ids_in{i}") for i in range(HOT_FIELDS)]
        hot_rows_in = sem("hot_rows_in")
        t_in = [sem(f"t_in{i}") for i in range(NBANK)]
        t_hi_ready = sem("t_hi_ready")
        t_lo_ready = sem("t_lo_ready")
        hot_ready = sem("hot_ready")
        zeros_ready = sem("zeros_ready")
        ident_ready = sem("ident_ready")
        k_hi_ready = sem("k_hi_ready")
        k_lo_ready = sem("k_lo_ready")
        k_lo_late = sem("k_lo_late")
        x_hi_ready = sem("x_hi_ready")
        x_lo_ready = sem("x_lo_ready")
        turned = sem("turned")
        x_ready = sem("x_ready")
        u_ready = sem("u_ready")
        prod_ready = sem("prod_ready")
        summed = sem("summed")
        z_ready = sem("z_ready")
        h1_done = sem("h1_done")
        h1_ready = sem("h1_ready")
        h2_done = sem("h2_done")
        h2_ready = sem("h2_ready")
        y_done = sem("y_done")
        y_ready = sem("y_ready")
        y_out = sem("y_out")

        steps, pool_steps = plan()
        rank = {n: i for i, n in enumerate(n for what, n in steps if what == "turn")}

        def turns_done(*turns):
            return max(rank[n] for n in turns) + 1

        def chunk_width(n):
            return CHUNK_GROUPS * GW if (n + 1) % CHUNKS else (CHUNK_GROUPS - 1) * GW + SW

        def columns(g):
            return (g % CHUNK_GROUPS) * GW, (P if g % GROUPS < COUPLE_GROUPS else E)

        def h1_ps(m):
            return (t_ps[0][:, :], t_ps[1][:, :], z_ps[0][:, :], u_ps[0][:, 0, :])[m]

        def wait_k_lo(eng, n):
            if n < VECTOR_CHUNKS:
                eng.wait_ge(k_lo_ready, n + 1)
            else:
                eng.wait_ge(k_lo_late, n - VECTOR_CHUNKS + 1)

        def wait_hot_turned(eng, h):
            eng.wait_ge(turned, turns_done(3 * 2 * (h // 2) + h % 2))

        def wait_dma_turned(eng, d):
            J = next(J for J in range(NJ) if not is_hot(J) and dma_index(J) == d)
            eng.wait_ge(turned, turns_done(3 * J, 3 * J + 1))

        def h1_early(pe, m):
            for kk in range(NBANK - 1):
                pe.matmul(h1_ps(m), w1_sb[:, kk, m * P:(m + 1) * P], z_sb[:, kk, :], start=kk == 0, stop=False)

        order = field_order()
        block = ctx.enter_context(nc.Block())

        @block.sync
        def _(sp):
            def load_table(h):
                sp.dma_start(t_raw[:, h % NBANK, :, :],
                             tables[order[4 * (h // 2) + h % 2]].rearrange("(p c) e -> p c e", c=HOT_CHUNKS)
                             ).then_inc(t_in[h % NBANK], 16)

            def load_hot_ids(i):
                sp.dma_start(hot_ids[:, i:i + 1, :],
                             hot_ids_d[:, i:i + 1, :].to_broadcast([HOT_ROWS, 1, B])).then_inc(hot_ids_in[i], 16)

            def load_chunk(n):
                at = (n // CHUNKS) * BANK_W + (n % CHUNKS) * CHUNK_GROUPS * GW
                if n >= KR:
                    wait_k_lo(sp, n - KR)
                for half in range(2):
                    sp.dma_start(k_raw[half * E:(half + 1) * E, n % KR, 0:chunk_width(n)],
                                 kern[:, at:at + chunk_width(n)]).then_inc(k_in[n % KR], 16)

            sp.dma_start(ids_sb[:, :, :], ids).then_inc(ids_in, 16)
            sp.dma_start(hot_rows[:, :], hot_rows_d).then_inc(hot_rows_in, 16)
            load_hot_ids(0)
            load_table(0)
            load_hot_ids(1)
            load_table(1)
            load_chunk(0)
            load_hot_ids(2)
            load_hot_ids(3)
            load_table(2)
            load_table(3)
            load_chunk(1)
            load_chunk(2)
            for n in range(KR, NBANK * CHUNKS):
                load_chunk(n)
                if n == WEIGHTS_AFTER:
                    sp.dma_start(w1_sb[:, :, :], w1).then_inc(weights_in, 16)
                    sp.dma_start(w3_sb[:, :], w3).then_inc(weights_in, 16)
                    sp.dma_start(b1_sb[:, :], b1).then_inc(weights_in, 16)
                    sp.dma_start(b2_sb[:, :], b2).then_inc(weights_in, 16)
            sp.wait_ge(x_lo_ready, NJ - HOT_STAGES)
            sp.dma_start(w2_sb, w2).then_inc(w2_in, 16)
            sp.wait_ge(y_ready, 1)
            sp.dma_start(out, y_sb).then_inc(y_out, 16)
            sp.wait_ge(y_out, 16)

        @block.gpsimd
        def _(pool):
            pool.wait_ge(ids_in, 16)
            for what, n, h in pool_steps:
                if what == "lookup":
                    d = dma_index(n)
                    if d >= XG:
                        pool.wait_ge(x_lo_ready, d - XG + 1)
                    for t in range(TB):
                        f = order[2 * n + h]
                        pool.indirect_dma_start(
                            gathered[:, d % XG, t, h * E:(h + 1) * E], None, tables[f],
                            bass.IndirectOffsetOnAxis(ap=ids_sb[:, t, f:f + 1], axis=0),
                        ).then_inc(field_in[n], 16)
                elif what == "chunk":
                    w = chunk_width(n)
                    pool.wait_ge(k_hi_ready, n + 1)
                    pool.tensor_tensor(k_lo[:, n % KS, 0:w], k_raw[:, n % KR, 0:w],
                                       k_hi[:, n % KS, 0:w].bitcast(F32), ALU.subtract).then_inc(k_lo_late, 1)

        @block.scalar
        def _(act):
            act.dma_start(ident, ident_d).then_inc(const_in, 16)
            act.dma_start(fold, fold_d).then_inc(const_in, 16)
            act.dma_start(sel_sb[:, :, :], sel).then_inc(const_in, 16)
            for what, n in steps:
                if what == "chunk":
                    w = chunk_width(n)
                    act.wait_ge(k_in[n % KR], 32 * (n // KR + 1))
                    if n >= KS:
                        act.wait_ge(u_ready, 2 * CHUNK_GROUPS * (n - KS + 1))
                    act.copy(k_hi[:, n % KS, 0:w], k_raw[:, n % KR, 0:w]).then_inc(k_hi_ready, 1)
                elif what == "table":
                    act.wait_ge(t_in[n % NBANK], 16 * (n // NBANK + 1))
                    if n >= 2:
                        wait_hot_turned(act, n - 2)
                    act.copy(t_split[:, n % 2, :, 0:E], t_raw[:, n % NBANK, :, :]).then_inc(t_hi_ready, 1)
                    if n == 1:
                        act.wait_ge(const_in, 3 * 16)
                        act.copy(ident_r[:, :], ident).then_inc(ident_ready, 1)
                        act.copy(fold_r[:, :], fold).then_inc(ident_ready, 1)
                elif what == "split":
                    d = dma_index(n)
                    act.wait_ge(field_in[n], 2 * TB * 16)
                    if d >= XS:
                        wait_dma_turned(act, d - XS)
                    act.copy(split[:, d % XS, :, :, 0:E],
                             gathered[:, d % XG, :, :].rearrange("p t (h e) -> p t h e", h=2)).then_inc(x_hi_ready, 1)
                elif what == "turn":
                    J, q = divmod(n, 3)
                    act.wait_ge(turned, rank[n] + 1)
                    to = moving[:, 2 * J + q, :] if q < 2 else factor[:, J, :]
                    act.copy(to, t_ps[rank[n] % 2][:, :]).then_inc(x_ready, 1)
                elif what == "dense":
                    g = GROUPS * n + COUPLE_GROUPS
                    act.wait_ge(summed, g - TS + 1)
                    act.dma_start(prod[E:E + 1, g % TS, :, :], dense[n]).then_inc(dense_in, 16)
                elif what == "bank":
                    act.wait_ge(summed, GROUPS * (n + 1))
                    act.copy(z_sb[:, n, :], z_ps[n % 2][:, :]).then_inc(z_ready, 1)
            act.wait_ge(weights_in, 4 * 16)
            for m in range(H1 // P):
                act.wait_ge(h1_done, m + 1)
                act.activation(h1_sb[:, m, :], h1_ps(m), ACT.Relu, bias=b1_sb[:, m:m + 1]).then_inc(h1_ready, 1)
            for m in range(H2 // P):
                act.wait_ge(h2_done, m + 1)
                act.activation(h2_sb[:, m, :], u_ps[1][:, m, :], ACT.Relu, bias=b2_sb[:, m:m + 1]).then_inc(h2_ready, 1)
            act.wait_ge(y_done, 1)
            act.copy(y_sb, t_ps[0][0:1, :]).then_inc(y_ready, 1)

        @block.vector
        def _(dve):
            dve.memset(zeros[:, :], 0.0).then_inc(zeros_ready, 1)
            for what, n in steps:
                if what == "chunk" and n < VECTOR_CHUNKS:
                    w = chunk_width(n)
                    dve.wait_ge(k_hi_ready, n + 1)
                    dve.tensor_tensor(k_lo[:, n % KS, 0:w], k_raw[:, n % KR, 0:w],
                                      k_hi[:, n % KS, 0:w].bitcast(F32), ALU.subtract).then_inc(k_lo_ready, 1)
                elif what == "table":
                    dve.wait_ge(t_hi_ready, n + 1)
                    dve.tensor_tensor(t_split[:, n % 2, :, E:2 * E], t_raw[:, n % NBANK, :, :],
                                      t_split[:, n % 2, :, 0:E].bitcast(F32), ALU.subtract).then_inc(t_lo_ready, 1)
                elif what == "hot":
                    dve.wait_ge(hot_rows_in, 16)
                    dve.wait_ge(hot_ids_in[n], 16)
                    if n >= 2:
                        wait_hot_turned(dve, n - 2)
                    for c in range(HOT_CHUNKS):
                        last = dve.tensor_scalar(hot[n % 2][:, c, :], hot_ids[:, n, :], hot_rows[:, c:c + 1], None,
                                                 ALU.is_equal)
                    last.then_inc(hot_ready, 1)
                elif what == "split":
                    d = dma_index(n)
                    dve.wait_ge(x_hi_ready, d + 1)
                    dve.tensor_tensor(split[:, d % XS, :, :, E:2 * E],
                                      gathered[:, d % XG, :, :].rearrange("p t (h e) -> p t h e", h=2),
                                      split[:, d % XS, :, :, 0:E].bitcast(F32), ALU.subtract).then_inc(x_lo_ready, 1)
                elif what == "group":
                    rows = P if n % GROUPS < COUPLE_GROUPS else E
                    for h, (m, js) in enumerate(group_blocks(n)):
                        bl = 2 * n + h
                        dve.wait_ge(u_ready, bl + 1)
                        dve.wait_ge(x_ready, turns_done(3 * m + 2, 3 * (m if rows == P else m + 1) + 2))
                        if n >= TS:
                            dve.wait_ge(summed, n - TS + 1)
                        if rows == P:
                            by = factor[:, m:m + 1, :].to_broadcast([P, 2, B])
                        else:
                            by = factor[0:rows, m:m + 2, :]
                        dve.tensor_tensor(prod[0:rows, n % TS, 2 * h:2 * h + 2, :], u_ps[bl % 2][0:rows, :, :],
                                          by, ALU.mult).then_inc(prod_ready, 1)

        @block.tensor
        def _(pe):
            turns = 0
            pe.wait_ge(zeros_ready, 1)
            for what, n in steps:
                if what == "warm":
                    if turns >= 2:
                        pe.wait_ge(x_ready, turns - 1)
                    for _ in range(n):
                        pe.matmul(t_ps[turns % 2][:, :], zeros[:, 0:P], zeros[:, :], start=True, stop=True)
                elif what == "turn":
                    turns = rank[n] + 1
                    J, q = divmod(n, 3)
                    if rank[n] >= 2:
                        pe.wait_ge(x_ready, rank[n] - 1)
                    to = t_ps[rank[n] % 2]
                    if n == 0:
                        pe.wait_ge(ident_ready, 2)
                    if q == 2:
                        pe.wait_ge(x_ready, turns_done(3 * J, 3 * J + 1))
                        pe.matmul(to[:, :], fold_r[:, E:3 * E], moving[:, 2 * J, :], start=True, stop=False)
                        last = pe.matmul(to[:, :], fold_r[:, 0:2 * E], moving[:, 2 * J + 1, :], start=False, stop=True)
                    elif is_hot(J):
                        h = 2 * hot_index(J) + q
                        pe.wait_ge(t_lo_ready, h + 1)
                        pe.wait_ge(hot_ready, h + 1)
                        for c in range(HOT_CHUNKS):
                            last = pe.matmul(to[:, :], t_split[:, h % 2, c, :], hot[h % 2][:, c, :],
                                             start=c == 0, stop=c == HOT_CHUNKS - 1)
                    else:
                        pe.wait_ge(x_lo_ready, dma_index(J) + 1)
                        for t in range(TB):
                            last = pe.transpose(to[:, t * P:(t + 1) * P].bitcast(F32R),
                                                split[:, dma_index(J) % XS, t, q, :], ident_r[:, :])
                    last.then_inc(turned, 1)
                elif what == "group":
                    k, r = divmod(n, GROUPS)
                    slot = n // CHUNK_GROUPS % KS
                    first, width = columns(n)
                    wait_k_lo(pe, n // CHUNK_GROUPS)
                    for h, (m, js) in enumerate(group_blocks(n)):
                        bl = 2 * n + h
                        pe.wait_ge(x_ready, turns_done(*(3 * (j // 2) + j % 2 for j in js)))
                        if bl >= 2:
                            pe.wait_ge(prod_ready, bl - 1)
                        for c, j in enumerate(js):
                            at = first + (2 * h + c) * width
                            pe.matmul(u_ps[bl % 2][0:width, c, :], k_hi[:, slot, at:at + width], moving[:, j, :],
                                      start=True, stop=False)
                            last = pe.matmul(u_ps[bl % 2][0:width, c, :], k_lo[:, slot, at:at + width], moving[:, j, :],
                                             start=False, stop=True)
                        last.then_inc(u_ready, 1)
                elif what == "sum":
                    k, r = divmod(n, GROUPS)
                    single = r == COUPLE_GROUPS
                    rows = E + 1 if single else P
                    if n == NG - 1:
                        pe.wait_ge(weights_in, 4 * 16)
                        pe.wait_ge(z_ready, NBANK - 1)
                        for m in range(H1 // P - 1):
                            h1_early(pe, m)
                    pe.wait_ge(prod_ready, 2 * n + 2)
                    if r == 0 and k >= 2:
                        pe.wait_ge(z_ready, k - 1)
                    if n == 0:
                        pe.wait_ge(const_in, 3 * 16)
                    if single:
                        pe.wait_ge(dense_in, 16 * (k + 1))
                    for c in range(STRIPS):
                        s = sel_sb[0:rows, 1, 1:33] if single else sel_sb[0:rows, 0, 30 - 2 * r:62 - 2 * r]
                        last = pe.matmul(z_ps[k % 2][32 * c:32 * c + 32, :], s, prod[0:rows, n % TS, c, :],
                                         start=r == 0, stop=single)
                    last.then_inc(summed, 1)
            h1_early(pe, H1 // P - 1)
            pe.wait_ge(z_ready, NBANK)
            for m in range(H1 // P):
                pe.matmul(h1_ps(m), w1_sb[:, NBANK - 1, m * P:(m + 1) * P], z_sb[:, NBANK - 1, :],
                          start=False, stop=True).then_inc(h1_done, 1)
            pe.wait_ge(w2_in, 16)
            last_kk = H1 // P - 1
            for kk, m in [(kk, m) for kk in range(last_kk) for m in range(H2 // P)]:
                pe.wait_ge(h1_ready, kk + 1)
                pe.matmul(u_ps[1][:, m, :], w2_sb[:, kk, m * P:(m + 1) * P], h1_sb[:, kk, :], start=kk == 0, stop=False)
            pe.wait_ge(h1_ready, H1 // P)
            for m in range(H2 // P):
                pe.matmul(u_ps[1][:, m, :], w2_sb[:, last_kk, m * P:(m + 1) * P], h1_sb[:, last_kk, :],
                          start=False, stop=True).then_inc(h2_done, 1)
            for kk in range(H2 // P):
                pe.wait_ge(h2_ready, kk + 1)
                last = pe.matmul(t_ps[0][0:1, :], w3_sb[:, kk:kk + 1], h2_sb[:, kk, :],
                                 start=kk == 0, stop=kk == H2 // P - 1)
            last.then_inc(y_done, 1)


def kernel(**inputs):
    import concourse.bacc as _bacc
    from concourse.bass_utils import run_bass_kernel_spmd as _run

    a = {k: np.asarray(v) for k, v in inputs.items()}
    order = field_order()
    kt = np.empty((E, NBANK * BANK_W // E, E), np.float32)
    for n, (i, j) in enumerate(pair for k in range(NBANK) for pair in bank_pairs(k)):
        i, j = order[i], order[j]
        one = a["L0_rec_kernel"][:, pair_index(*sorted((i, j))), :]
        kt[:, n, :] = one if i < j else one.T
    kt = kt.reshape(E, NBANK * BANK_W)
    rows = np.concatenate([z_rows(k) for k in range(NBANK)])

    sel = np.zeros((P, 2, 62), np.float32)
    sel[:E, 0, 30] = 1
    sel[E:, 0, 31] = 1
    sel[:E, 1, 31] = 1
    sel[E, 1, 32] = 1

    fold = np.zeros((P, 3 * E), np.float32)
    fold[:, E:2 * E] = np.tile(np.eye(E), (2, 1))
    hot_rows = (HOT_CHUNKS * np.arange(HOT_ROWS)[:, None] + np.arange(HOT_CHUNKS)).astype(np.float32)
    hot_fields = [order[2 * J + h] for J in range(NJ) if is_hot(J) for h in range(2)]

    arrays = {
        "fold": fold, "hot_rows": hot_rows,
        "hot_ids": a["ids"][:, hot_fields].T[None],
        "ids": a["ids"].reshape(TB, P, F).transpose(1, 0, 2),
        **{f"tbl_{f}": a[f"tbl_{f}"] for f in range(F)},
        "kern": kt,
        "dense": a["dense_ctx"].T.reshape(NBANK, 1, STRIPS, B),
        "w1": a["W_top1"][rows].reshape(NBANK, P, H1).transpose(1, 0, 2),
        "b1": a["b_top1"].reshape(H1 // P, P).T,
        "w2": a["W_top2"].reshape(H1 // P, P, H2).transpose(1, 0, 2),
        "b2": a["b_top2"].reshape(H2 // P, P).T,
        "w3": a["W_top3"].reshape(H2 // P, P).T,
        "sel": sel, "ident": np.eye(P, dtype=np.float32),
    }
    arrays = {f"in_{k}": np.ascontiguousarray(v) for k, v in arrays.items()}
    nc = _bacc.Bacc("TRN2", target_bir_lowering=False, num_devices=1)
    ap = {k: nc.dram_tensor(k, v.shape, mybir.dt.from_np(v.dtype), kind="ExternalInput").ap() for k, v in arrays.items()}
    out = nc.dram_tensor("out_y", (1, B), mybir.dt.float32, kind="ExternalOutput").ap()
    build(nc, ap["in_ids"], [ap[f"in_tbl_{f}"] for f in range(F)], ap["in_kern"], ap["in_dense"], ap["in_w1"],
          ap["in_b1"], ap["in_w2"], ap["in_b2"], ap["in_w3"], ap["in_sel"], ap["in_ident"], ap["in_fold"],
          ap["in_hot_ids"], ap["in_hot_rows"], out)
    r = _run(nc, [arrays], core_ids=[0])
    return r.results[0]["out_y"].reshape(B, 1)
```
